# Optimizing a Trainium2 kernel written in Bass

```python
import numpy as np
import jax
import jax.numpy as jnp

def _softmax(x, axis=-1):
    return jax.nn.softmax(x, axis=axis)

def _gelu(x):
    return jax.nn.gelu(x, approximate=True)

def _silu(x):
    return jax.nn.silu(x)

def _sigmoid(x):
    return jax.nn.sigmoid(x)

def _layernorm(x, axis=-1, eps=1e-05):
    m = jnp.mean(x, axis=axis, keepdims=True)
    v = jnp.var(x, axis=axis, keepdims=True)
    return (x - m) / jnp.sqrt(v + eps)

def _scatter_add(tgt, idx, src, axis=0):
    return tgt.at[idx].add(src)

def _segment_sum(src, seg, n):
    return jax.ops.segment_sum(src, seg, n)
kernel_name = 'mk_perceiver_d1_seqx_r2_71a59c'

def setup_inputs(seed: int=0):
    np.random.seed(seed)
    _w = jnp.asarray

    def _rec_inputs():
        import jax
        import jax.numpy as jnp
        _rk = jax.random.key(seed)
        x = -0.000125 + 0.9999 * jax.random.normal(jax.random.fold_in(_rk, 1), (16, 64, 1024), jnp.float32)
        _lenS = 64 - jax.random.randint(jax.random.fold_in(_rk, 7), (16,), 0, max(1, 64 // 4) + 1, jnp.int32)
        _lenS2 = 1601 - jax.random.randint(jax.random.fold_in(_rk, 8), (16,), 0, max(1, 1601 // 4) + 1, jnp.int32)
        _ctx_2048P = jax.random.normal(jax.random.fold_in(_rk, 11), (16, 16, 1024), jnp.float32)
        _ctx_2048c = jax.random.dirichlet(jax.random.fold_in(_rk, 511), 0.3 * jnp.ones((16,), jnp.float32), (16, 1601))
        _ctx_2048t = jnp.einsum('bsk,bkd->bsd', _ctx_2048c, _ctx_2048P)
        _ctx_2048t = _ctx_2048t * jax.lax.rsqrt(jnp.mean(jnp.square(_ctx_2048t)) + 1e-12) * 0.953939
        ctx_2048 = -1.52775e-05 + 0.999936 * (_ctx_2048t + 0.3 * jax.random.normal(jax.random.fold_in(_rk, 611), (16, 1601, 1024), jnp.float32))
        return (x, ctx_2048)
    x, ctx_2048 = _rec_inputs()

    def _L0_xattn_setup():
        import jax, jax.numpy as jnp
        import numpy as np
        BN_EPS = 1e-05
        RENORM_EPS = 1e-09
        B, C, M, N = (128, 64, 64, 1024)
        key = jax.random.key(seed)
        k1, k2, k3, k4, k5 = jax.random.split(key, 5)
        x1 = jax.random.normal(k1, (B, C, N), dtype=jnp.float32)
        x2 = jax.random.normal(k2, (B, M, N), dtype=jnp.float32)
        x1_2 = jax.random.normal(k3, (B, M, N), dtype=jnp.float32)
        conv_w = jax.random.normal(k4, (C, C), dtype=jnp.float32) * (1.0 / np.sqrt(C))
        conv_b = jax.random.normal(k5, (C,), dtype=jnp.float32) * 0.01
        bn_gamma = jnp.ones((C,), dtype=jnp.float32)
        bn_beta = jnp.zeros((C,), dtype=jnp.float32)
        return {'x1': x1, 'x2': x2, 'x1_2': x1_2, 'conv_w': conv_w, 'conv_b': conv_b, 'bn_gamma': bn_gamma, 'bn_beta': bn_beta}
    _L0_xattn_all = _L0_xattn_setup()
    _L0_xattn_in = {k: v for k, v in _L0_xattn_all.items() if k in ('conv_w', 'conv_b', 'bn_gamma', 'bn_beta')}
    del _L0_xattn_all

    def _L0_attn_setup():
        import math
        import jax, jax.numpy as jnp
        import numpy as np
        B, T, E = (2, 1024, 1024)
        NUM_HEADS = 16
        H = NUM_HEADS // 2
        D = E // NUM_HEADS
        DEPTH = 12
        LAMBDA_INIT = 0.8 - 0.6 * math.exp(-0.3 * DEPTH)
        EPS = 1e-05

        def _forward(x, Wq, Wk, Wv, Wo, lq1, lk1, lq2, lk2, g):
            Bz, Tl, _ = x.shape
            q = (x @ Wq).reshape(Bz, Tl, H, 2, D)
            k = (x @ Wk).reshape(Bz, Tl, H, 2, D)
            v = (x @ Wv).reshape(Bz, Tl, H, 2 * D)
            scale = D ** (-0.5)
            causal = jnp.tril(jnp.ones((Tl, Tl), dtype=bool))

            def attend(qc, kc):
                s = jnp.einsum('bthd,bshd->bhts', qc, kc) * scale
                s = jnp.where(causal, s, -jnp.inf)
                a = jax.nn.softmax(s, axis=-1)
                return jnp.einsum('bhts,bshe->bthe', a, v)
            o1 = attend(q[..., 0, :], k[..., 0, :])
            o2 = attend(q[..., 1, :], k[..., 1, :])
            lam = jnp.exp(jnp.sum(lq1 * lk1)) - jnp.exp(jnp.sum(lq2 * lk2)) + LAMBDA_INIT
            o = o1 - lam * o2
            o = o * jax.lax.rsqrt(jnp.mean(o * o, axis=-1, keepdims=True) + EPS) * g
            o = o * (1.0 - LAMBDA_INIT)
            return o.reshape(Bz, Tl, E) @ Wo
        key = jax.random.key(seed)
        ks = jax.random.split(key, 10)
        sc = lambda k, shape, std: jax.random.normal(k, shape, dtype=jnp.float32) * std
        return {'x': jax.random.normal(ks[0], (B, T, E), dtype=jnp.float32), 'Wq': sc(ks[1], (E, E), 0.02), 'Wk': sc(ks[2], (E, E), 0.02), 'Wv': sc(ks[3], (E, E), 0.02), 'Wo': sc(ks[4], (E, E), 0.02), 'lambda_q1': sc(ks[5], (D,), 0.1), 'lambda_k1': sc(ks[6], (D,), 0.1), 'lambda_q2': sc(ks[7], (D,), 0.1), 'lambda_k2': sc(ks[8], (D,), 0.1), 'g': jnp.ones((2 * D,), dtype=jnp.float32)}
    _L0_attn_all = _L0_attn_setup()
    _L0_attn_in = {k: v for k, v in _L0_attn_all.items() if k in ('Wq', 'Wk', 'Wv', 'Wo', 'lambda_q1', 'lambda_k1', 'lambda_q2', 'lambda_k2', 'g')}
    del _L0_attn_all

    def _L0_ffn_setup():
        import jax, jax.numpy as jnp
        import numpy as np
        THRESHOLD = 0.05
        ACT_BITS = 4
        QMAX = 2 ** (ACT_BITS - 1) - 1
        EPS = 1e-08

        def ternarize(W, threshold):
            absW = jnp.abs(W)
            delta = threshold * jnp.max(absW)
            mask = absW > delta
            n = jnp.maximum(jnp.sum(mask), 1)
            alpha = jnp.sum(jnp.where(mask, absW, 0.0)) / n
            Wt = alpha * jnp.sign(W) * mask
            return W + jax.lax.stop_gradient(Wt - W)

        def ternary_linear(x, W, b, threshold=THRESHOLD):
            Wq = ternarize(W, threshold)
            return jnp.einsum('bsd,hd->bsh', x, Wq) + b

        def fp4_activation(x):
            scale = jnp.max(jnp.abs(x)) / QMAX + EPS
            q = jnp.clip(jnp.round(x / scale), -QMAX, QMAX) * scale
            return x + jax.lax.stop_gradient(q - x)
        key = jax.random.key(seed)
        k1, k2, k3, k4, k5 = jax.random.split(key, 5)
        B, S, D, H = (2, 2048, 1024, 4096)
        x = jax.random.normal(k1, (B, S, D), dtype=jnp.float32)
        W1 = jax.random.normal(k2, (H, D), dtype=jnp.float32) * (1.0 / np.sqrt(D))
        b1 = jax.random.normal(k3, (H,), dtype=jnp.float32) * 0.02
        W2 = jax.random.normal(k4, (D, H), dtype=jnp.float32) * (1.0 / np.sqrt(H))
        b2 = jax.random.normal(k5, (D,), dtype=jnp.float32) * 0.02
        return {'x': x, 'W1': W1, 'b1': b1, 'W2': W2, 'b2': b2}
    _L0_ffn_all = _L0_ffn_setup()
    _L0_ffn_in = {k: v for k, v in _L0_ffn_all.items() if k in ('W1', 'b1', 'W2', 'b2')}
    del _L0_ffn_all
    return {'x': x, 'ctx_2048': ctx_2048, 'L0_xattn_conv_w': _L0_xattn_in['conv_w'], 'L0_xattn_conv_b': _L0_xattn_in['conv_b'], 'L0_xattn_bn_gamma': _L0_xattn_in['bn_gamma'], 'L0_xattn_bn_beta': _L0_xattn_in['bn_beta'], 'L0_attn_Wq': _L0_attn_in['Wq'], 'L0_attn_Wk': _L0_attn_in['Wk'], 'L0_attn_Wv': _L0_attn_in['Wv'], 'L0_attn_Wo': _L0_attn_in['Wo'], 'L0_attn_lambda_q1': _L0_attn_in['lambda_q1'], 'L0_attn_lambda_k1': _L0_attn_in['lambda_k1'], 'L0_attn_lambda_q2': _L0_attn_in['lambda_q2'], 'L0_attn_lambda_k2': _L0_attn_in['lambda_k2'], 'L0_attn_g': _L0_attn_in['g'], 'L0_ffn_W1': _L0_ffn_in['W1'], 'L0_ffn_b1': _L0_ffn_in['b1'], 'L0_ffn_W2': _L0_ffn_in['W2'], 'L0_ffn_b2': _L0_ffn_in['b2']}

def reference(x, ctx_2048, L0_xattn_conv_w, L0_xattn_conv_b, L0_xattn_bn_gamma, L0_xattn_bn_beta, L0_attn_Wq, L0_attn_Wk, L0_attn_Wv, L0_attn_Wo, L0_attn_lambda_q1, L0_attn_lambda_k1, L0_attn_lambda_q2, L0_attn_lambda_k2, L0_attn_g, L0_ffn_W1, L0_ffn_b1, L0_ffn_W2, L0_ffn_b2):
    import jax
    import jax.numpy as jnp

    def _L0_xattn_ref(x1, x2, x1_2, conv_w, conv_b, bn_gamma, bn_beta):
        import jax, jax.numpy as jnp
        import numpy as np
        BN_EPS = 1e-05
        RENORM_EPS = 1e-09
        B, C, M, N = (128, 64, 64, 1024)
        energy = jnp.einsum('bcn,bmn->bcm', x1, x2)
        attn = jax.nn.softmax(energy, axis=-1)
        attn = attn / (RENORM_EPS + attn.sum(axis=1, keepdims=True))
        x_r = jnp.einsum('bcm,bmn->bcn', attn, x1_2)
        t = x1 - (jnp.einsum('oc,bcn->bon', conv_w, x_r) + conv_b[None, :, None])
        mean = t.mean(axis=(0, 2), keepdims=True)
        var = t.var(axis=(0, 2), keepdims=True)
        t_hat = (t - mean) * jax.lax.rsqrt(var + BN_EPS)
        t_bn = t_hat * bn_gamma[None, :, None] + bn_beta[None, :, None]
        x_r_out = jax.nn.relu(t_bn)
        return x1 + x_r_out

    def _L0_attn_ref(x, Wq, Wk, Wv, Wo, lambda_q1, lambda_k1, lambda_q2, lambda_k2, g):
        import math
        import jax, jax.numpy as jnp
        import numpy as np
        B, T, E = (2, 1024, 1024)
        NUM_HEADS = 16
        H = NUM_HEADS // 2
        D = E // NUM_HEADS
        DEPTH = 12
        LAMBDA_INIT = 0.8 - 0.6 * math.exp(-0.3 * DEPTH)
        EPS = 1e-05

        def _forward(x, Wq, Wk, Wv, Wo, lq1, lk1, lq2, lk2, g):
            Bz, Tl, _ = x.shape
            q = (x @ Wq).reshape(Bz, Tl, H, 2, D)
            k = (x @ Wk).reshape(Bz, Tl, H, 2, D)
            v = (x @ Wv).reshape(Bz, Tl, H, 2 * D)
            scale = D ** (-0.5)
            causal = jnp.tril(jnp.ones((Tl, Tl), dtype=bool))

            def attend(qc, kc):
                s = jnp.einsum('bthd,bshd->bhts', qc, kc) * scale
                s = jnp.where(causal, s, -jnp.inf)
                a = jax.nn.softmax(s, axis=-1)
                return jnp.einsum('bhts,bshe->bthe', a, v)
            o1 = attend(q[..., 0, :], k[..., 0, :])
            o2 = attend(q[..., 1, :], k[..., 1, :])
            lam = jnp.exp(jnp.sum(lq1 * lk1)) - jnp.exp(jnp.sum(lq2 * lk2)) + LAMBDA_INIT
            o = o1 - lam * o2
            o = o * jax.lax.rsqrt(jnp.mean(o * o, axis=-1, keepdims=True) + EPS) * g
            o = o * (1.0 - LAMBDA_INIT)
            return o.reshape(Bz, Tl, E) @ Wo
        return _forward(x, Wq, Wk, Wv, Wo, lambda_q1, lambda_k1, lambda_q2, lambda_k2, g)

    def _L0_ffn_ref(x, W1, b1, W2, b2):
        import jax, jax.numpy as jnp
        import numpy as np
        THRESHOLD = 0.05
        ACT_BITS = 4
        QMAX = 2 ** (ACT_BITS - 1) - 1
        EPS = 1e-08

        def ternarize(W, threshold):
            absW = jnp.abs(W)
            delta = threshold * jnp.max(absW)
            mask = absW > delta
            n = jnp.maximum(jnp.sum(mask), 1)
            alpha = jnp.sum(jnp.where(mask, absW, 0.0)) / n
            Wt = alpha * jnp.sign(W) * mask
            return W + jax.lax.stop_gradient(Wt - W)

        def ternary_linear(x, W, b, threshold=THRESHOLD):
            Wq = ternarize(W, threshold)
            return jnp.einsum('bsd,hd->bsh', x, Wq) + b

        def fp4_activation(x):
            scale = jnp.max(jnp.abs(x)) / QMAX + EPS
            q = jnp.clip(jnp.round(x / scale), -QMAX, QMAX) * scale
            return x + jax.lax.stop_gradient(q - x)
        h = ternary_linear(x, W1, b1)
        h = jax.nn.gelu(h, approximate=False)
        y = ternary_linear(h, W2, b2)
        return fp4_activation(y)
    x = x + _L0_xattn_ref(_layernorm(x, axis=-1), ctx_2048, ctx_2048, L0_xattn_conv_w, L0_xattn_conv_b, L0_xattn_bn_gamma, L0_xattn_bn_beta)
    x = x + _L0_attn_ref(_layernorm(x, axis=-1), L0_attn_Wq, L0_attn_Wk, L0_attn_Wv, L0_attn_Wo, L0_attn_lambda_q1, L0_attn_lambda_k1, L0_attn_lambda_q2, L0_attn_lambda_k2, L0_attn_g)
    x = x + _L0_ffn_ref(_layernorm(x, axis=-1), L0_ffn_W1, L0_ffn_b1, L0_ffn_W2, L0_ffn_b2)
    return x

_drawn_inputs = setup_inputs


def setup_inputs(seed=0):
    import zlib

    import numpy as np

    out = dict(_drawn_inputs(seed))
    spreads = {'L0_xattn_bn_gamma': (1.0, 0.2), 'L0_xattn_bn_beta': (0.0, 0.1), 'L0_attn_g': (1.0, 0.6)}
    factors = {'L0_xattn_conv_b': 8.0,
     'L0_attn_lambda_q1': 8.0,
     'L0_attn_lambda_k1': 3.048,
     'L0_attn_lambda_q2': 3.983,
     'L0_attn_lambda_k2': 5.141}
    for name, (base, spread) in spreads.items():
        noise = np.random.default_rng([zlib.crc32(name.encode()), seed]).standard_normal(out[name].shape)
        drawn = base * np.exp(spread * noise) if base else spread * noise
        out[name] = jnp.asarray(drawn.astype(out[name].dtype))
    for name, factor in factors.items():
        out[name] = (out[name] * factor).astype(out[name].dtype)
    return out
```

```python
from contextlib import ExitStack
import math

import numpy as np
import concourse.bass as bass
from concourse import mybir

F32 = mybir.dt.float32
F16 = mybir.dt.float16
ALU = mybir.AluOpType
ACT = mybir.ActivationFunctionType
AX = mybir.AxisListType
RED = bass.bass_isa.ReduceOp

P = 128
B, C, N = 16, 64, 1024
M = 1601
NT = B * C // P
NC = N // P
BANK = 512
G = (M + BANK - 1) // BANK
MT = (M + P - 1) // P
TAIL = M - (MT - 1) * P
STEPS = 4 * (G - 2) + 1
U_X1, U_AT = 4 * STEPS, 4 * STEPS + 2
UNITS = U_AT + G
TB = 3
USES = UNITS // TB
assert UNITS % (2 * TB) == 0
ORDER = (1, 2, 3, 0)
LAST_ORDER = (0, 1, 3, 2)
H = 8
D = 64
HID = 4096
HC = HID // P
WT = HID * N // P // 1024
EPS = 1e-5
LAMBDA_INIT = 0.8 - 0.6 * math.exp(-0.3 * 12)
X_SCALE = 1024.0
H_RANGE = 32000.0
ROUND = 1.5 * 2.0 ** 23
QMAX = 7.0
POOL_TILES = (1, 4)

C_ID, C_PAIR, C_MASK, C_ONE, C_W = 0, P, 2 * P, 2 * P + D, 2 * P + D + P


def constants():
    c = np.zeros((P, C_W), np.float32)
    i = np.arange(P)
    c[:, C_ID:C_ID + P] = np.eye(P)
    c[:, C_PAIR:C_PAIR + P] = 0.5 * (i[:, None] % C == i[None, :] % C)
    c[:, C_MASK:C_MASK + D] = np.where(np.arange(D)[None, :] <= i[:, None] % C, 0.0, -1e30)
    c[:, C_ONE:C_ONE + P] = 1.0
    return c


def build(nc, x, ctx, ctx0T, conv_wT, conv_b, bn_gamma, bn_beta, wqkv, wo, lambdas, g_in, w1t, b1, w2t, b2, consts, out):
    with ExitStack() as stack:
        sem = lambda name: stack.enter_context(nc.semaphore(name))
        BASE = nc.sbuf_base + (-nc.sbuf_base) % 32

        def sb(name, shape, at, dt=F32):
            return nc.alloc_sbuf_tensor_at(name, shape, dt, offset=BASE + at)

        KB = 1024
        ctx_sb = sb("ctx_sb", [P, 2, MT, N], 0)
        ctxT0 = sb("ctxT0", [P, 2, NC, BANK], 104 * KB)
        ctxT = sb("ctxT", [P, 2, 4, BANK], 136 * KB)
        x_t = sb("x_t", [P, N], 152 * KB)
        x1s = sb("x1s", [P, 2, N], 156 * KB)
        x1T = sb("x1T", [P, NC, P], 164 * KB)
        prob = sb("prob", [P, M], 168 * KB)
        xr_sb = sb("xr_sb", [P, N], 168 * KB)
        attnT = sb("attnT", [P, MT, P], 168 * KB + 6432)
        wa_buf = sb("wa_buf", [P, 4, 1024], 184 * KB)
        tok = sb("tok", [P, NT, N], 120 * KB)
        xo = sb("xo", [P, NT, N], 0)
        x2T = sb("x2T", [P, NC, NT * P], 32 * KB)
        oT = sb("oT", [P, H, NT * P], 64 * KB)
        wqkv_sb = sb("wqkv_sb", [P, 3, NC, P], 104 * KB)
        sm = sb("sm", [P, 2, NT, D], 116 * KB)
        wo_sb = sb("wo_sb", [P, NC, N], 120 * KB)
        qT = sb("qT", [P, NT * P], 152 * KB)
        kT = sb("kT", [P, NT * P], 156 * KB)
        v_sb = sb("v_sb", [P, NT, P], 160 * KB)
        a_bd = sb("a_bd", [P, NT, P], 164 * KB)
        aT = sb("aT", [P, NT, P], 168 * KB)
        o_sq = sb("o_sq", [P, NT, P], 172 * KB)
        o_n = sb("o_n", [P, NT, P], 176 * KB)
        w_buf = sb("w_buf", [P, 2, 1024], 184 * KB)
        t_out = sb("t_out", [P, 2, 1024], 192 * KB, F16)
        xs = sb("xs", [P, 2, N], 196 * KB)
        x3h = sb("x3h", [P, NC, NT * P], 32 * KB, F16)
        x3l = sb("x3l", [P, NC, NT * P], 48 * KB, F16)
        h_hi = sb("h_hi", [P, HC, NT * P], 64 * KB, F16)
        h_lo = sb("h_lo", [P, HC, NT * P], 128 * KB, F16)
        t_buf = sb("t_buf", [P, 4, 1024], 192 * KB, F16)
        g_buf = sb("g_buf", [P, 2, BANK], 200 * KB)
        b2_bc = sb("b2_bc", [P, N], 200 * KB)
        y = sb("y", [P, NT, N], 32 * KB)
        at = [204 * KB]

        def small(name, shape):
            n = 4 * int(np.prod(shape[1:]))
            t = sb(name, shape, at[0])
            at[0] += n + (-n) % 32
            return t

        cst = small("cst", [P, C_W])
        conv_bd = small("conv_bd", [P, P])
        cols = small("cols", [P, 4])
        mx4 = small("mx4", [P, 4])
        nmx = small("nmx", [P, 1])
        zs = small("zs", [P, 3])
        cs = small("cs", [P, 4 * 8])
        st = small("st", [P, 8, 6])
        mv = small("mv", [P, NT, 2])
        rs = small("rs", [P, 3, NT])
        t8 = small("t8", [P, NT])
        bn = sb("bn", [P, NT, 2, 6], 183 * KB + 576)
        bnm = small("bnm", [P, 8])
        wmx = sb("wmx", [P, 2, WT], 183 * KB + 320)
        thr = small("thr", [P, 3, 2])
        wacc = small("wacc", [P, 2, 2, 4])
        wtot = small("wtot", [P, 4])
        lam_sb = sb("lam_sb", [P, 4 * D + 8], 182 * KB)
        o_cnt = sb("o_cnt", [P, 1024], 180 * KB, F16)
        w_junk = sb("w_junk", [P, 1024], 196 * KB, F16)
        neg_lam = small("neg_lam", [P, 1])
        sx = sb("sx", [P, 4, 2 * NT], 183 * KB + 64)
        al = small("al", [P, 8])
        b1_sb = small("b1_sb", [P, HC])
        ym = small("ym", [P, 24])
        assert BASE + at[0] <= nc.sbuf_usable_end, (at[0], nc.sbuf_usable_end - BASE)

        ident = cst[:, C_ID:C_ID + P]
        ps = stack.enter_context(nc.psum_tensor("ps", [P, 8 * BANK], F32))
        bank = lambda k, n=BANK: ps[:, k * BANK:k * BANK + n]

        s_dram = nc.dram_tensor("s_dram", [NT, P, N], F32).ap()
        n_dram = nc.dram_tensor("n_dram", [NT, P, N], F32).ap()
        t1_dram = nc.dram_tensor("t1_dram", [N, HID], F16).ap()
        t2_dram = nc.dram_tensor("t2_dram", [HID, N], F16).ap()
        x_v = x.rearrange("(t p) n -> t p n", p=P)
        out_v = out.rearrange("(t p) n -> p t n", p=P)
        tiles = lambda w: w.rearrange("(p a) (b n) -> p (a b) n", p=P, n=1024)
        w_v = [tiles(w1t), tiles(w2t)]
        t_v = [tiles(t1_dram), tiles(t2_dram)]
        t1_v = t1_dram.rearrange("(c p) (h f) -> h p c f", p=P, f=P)
        t2_v = t2_dram.rearrange("(h p) n -> h p n", p=P)

        flat = lambda a: a.rearrange("p a n -> p (a n)")
        flat4 = lambda a: a.rearrange("p a b n -> p (a b n)")

        def pick(t, i):
            return t[:, bass.ds(i, 1), :].rearrange("p a n -> p (a n)")

        passed = sem("passed")
        cst_in, small_in, x_in, ctxT0_in = sem("cst_in"), sem("small_in"), sem("x_in"), sem("ctxT0_in")
        first_T0 = [sem(f"first_T0_{k}") for k in range(4)]
        first_g = [[sem(f"first_g{g}_{k}") for k in range(4)] for g in (1, 2)]
        ctx_in = [sem(f"ctx_in{g}") for g in range(G)]
        w_in = [sem(f"w_in{i}") for i in range(4)]
        w_used = sem("w_used")
        vec = sem("vec")
        var_ready, root_ready = sem("var_ready"), sem("root_ready")
        x1s_ready, s_ready, s_stored = sem("x1s_ready"), sem("s_ready"), sem("s_stored")
        n_stored = sem("n_stored")
        tr_ready = sem("tr_ready")
        tr_free = [sem(f"tr_free{k}") for k in range(TB)]
        e_done, e0_done = sem("e_done"), sem("e0_done")
        nmax_ready, exp_done, attn_ready = sem("nmax_ready"), sem("exp_done"), sem("attn_ready")
        pv_done = sem("pv_done")
        xr_done = sem("xr_done")
        xr_act, xr_dve = sem("xr_act"), sem("xr_dve")
        cv_done, cv_free = sem("cv_done"), sem("cv_free")
        n_in = sem("n_in")
        bn_st, bn_part, bn_avg, bn_ready = sem("bn_st"), sem("bn_part"), sem("bn_avg"), sem("bn_ready")
        wmax_ready, wmax_all = sem("wmax_ready"), sem("wmax_all")
        s_in = [sem(f"s_in{i}") for i in range(2)]
        relu_done, xs_ready = sem("relu_done"), sem("xs_ready")
        x2_tr, x2_act, x2_dve = sem("x2_tr"), sem("x2_act"), sem("x2_dve")
        wqkv_in = [sem(f"wqkv_in{i}") for i in range(3)]
        wo_in = sem("wo_in")
        q_done, k_done, v_done, s_done = sem("q_done"), sem("k_done"), sem("v_done"), sem("s_done")
        at_done, o_done, ot_done = sem("at_done"), sem("o_done"), sem("ot_done")
        q_out = [sem("q_act"), sem("q_dve")]
        k_out = [sem("k_act"), sem("k_dve")]
        v_out = [sem("v_act"), sem("v_dve")]
        a_out = [sem("a_act"), sem("a_dve")]
        oT_out = [sem("oT_act"), sem("oT_dve")]
        sh_ready, p_ready, a_ready = sem("sh_ready"), sem("p_ready"), sem("a_ready")
        sq_done, on_ready = sem("sq_done"), sem("on_ready")
        lam_ready, lam_exp, tz = sem("lam_ready"), sem("lam_exp"), sem("tz")
        w2_in = [sem(f"w2_in{i}") for i in range(2)]
        t_ready, t_counted = sem("t_ready"), sem("t_counted")
        t_stored = [sem(f"t_stored{i}") for i in range(2)]
        pr_done, x3_done, x3_tr, x3_hi, x3_lo = sem("pr_done"), sem("x3_done"), sem("x3_tr"), sem("x3_hi"), sem("x3_lo")
        tot_ready, tot_sum, al_ready = sem("tot_ready"), sem("tot_sum"), sem("al_ready")
        bmax_ready, bmax_all = sem("bmax_ready"), sem("bmax_all")
        t_in = [sem(f"t_in{k}") for k in range(4)]
        b2_in = sem("b2_in")
        h_done, g_ready, h_high, h_ready = sem("h_done"), sem("g_ready"), sem("h_high"), sem("h_ready")
        t2_used, y_done, y_out, y_max, y_all = sem("t2_used"), sem("y_done"), sem("y_out"), sem("y_max"), sem("y_all")
        clip_ready, whole_ready, pool_ready = sem("clip_ready"), sem("whole_ready"), sem("pool_ready")
        z_ready, q_ready, d_vec, out_stored = sem("z_ready"), sem("q_ready"), sem("d_vec"), sem("out_stored")

        def apart(eng):
            eng.sem_inc(passed, 1)

        class Own:

            def __init__(self, eng, s, start=0):
                self.eng, self.s, self.start, self.n = eng, s, start, 0

            def done(self, ins):
                ins.then_inc(self.s, 1)
                self.n += 1
                self.eng.wait_ge(self.s, self.start + self.n)

        block = stack.enter_context(nc.Block())

        @block.sync
        def _(sp):
            sp.dma_start(x_t[:, :], x_v[0]).then_inc(x_in, 16)
            sp.dma_start(cst[:, :], consts).then_inc(cst_in, 16)

            def load_ctx(p, g):
                t0, nt = 4 * g, (4 if g < G - 1 else 1)
                for b in range(2):
                    src = ctx[bass.ds(2 * p + b, 1), t0 * P:min(M, (t0 + nt) * P), :]
                    if nt > 1:
                        sp.dma_start(ctx_sb[:, b, t0:t0 + nt, :], src.rearrange("a (t p) n -> p (a t) n", p=P))\
                          .then_inc(ctx_in[g], 16)
                    else:
                        sp.dma_start(ctx_sb[0:TAIL, b, t0, :], src.rearrange("a p n -> p (a n)"))\
                          .then_inc(ctx_in[g], 16)

            def load_ctxT0(p):
                for b in range(2):
                    sp.dma_start(ctxT0[:, b, :, :], ctx0T[bass.ds(2 * p + b, 1)].rearrange("a (c p) m -> p (a c) m", p=P))\
                      .then_inc(ctxT0_in, 16)

            for k in range(4):
                for b in range(2):
                    sp.dma_start(ctxT0[:, b, 2 * k:2 * k + 2, :],
                                 ctx0T[b, 2 * k * P:(2 * k + 2) * P, :].rearrange("(c p) m -> p c m", p=P))\
                      .then_inc(first_T0[k], 16)
            sp.wait_ge(s_ready, 1)
            sp.dma_start(s_dram[0], x_t[:, :]).then_inc(s_stored, 16)
            for g in (1, 2):
                for k in range(4):
                    for b in range(2):
                        f = slice(2 * k * P, (2 * k + 2) * P)
                        sp.dma_start(ctx_sb[:, b, 4 * g:4 * g + 4, f],
                                     ctx[b, g * BANK:(g + 1) * BANK, f].rearrange("(t p) n -> p t n", p=P))\
                          .then_inc(first_g[g - 1][k], 16)
                if g == 1:
                    sp.wait_ge(s_stored, 16)
                    sp.dma_start(x_t[:, :], x_v[1]).then_inc(x_in, 16)
            load_ctx(0, 3)
            sp.wait_ge(e0_done, 1)
            load_ctxT0(1)
            for i in range(4):
                sp.dma_start(wa_buf[:, i, :], w_v[0][:, i, :]).then_inc(w_in[i], 16)
            load_ctx(0, 0)
            for b in range(2):
                r = slice(C * b, C * b + C)
                sp.dma_start(conv_bd[r, r], conv_wT).then_inc(small_in, 16)
                for i, a in enumerate((conv_b, bn_gamma, bn_beta)):
                    sp.dma_start(cols[r, i:i + 1], a.rearrange("(p a) -> p a", a=1)).then_inc(small_in, 16)
            sp.dma_start(cols[:, 3:4], g_in.rearrange("(p a) -> p a", a=1)).then_inc(small_in, 16)
            sp.dma_start(b1_sb[:, :], b1).then_inc(small_in, 16)
            sp.dma_start(lam_sb[:, 0:4 * D], lambdas.partition_broadcast(P)).then_inc(small_in, 16)

            def load_a(p, u, nxt):
                for n, g in enumerate(ORDER):
                    sp.wait_ge(pv_done, G * p + (n + 1 - G))
                    apart(sp)
                    if g == 0:
                        sp.wait_ge(cv_free, 2 * p)
                        apart(sp)
                        sp.dma_start(n_dram[bass.ds(p - 1, 1)].rearrange("a p n -> p (a n)"), x1s[:, u, :])\
                          .then_inc(n_stored, 16)
                    if g == 0 and nxt:
                        sp.wait_ge(e0_done, p + 1)
                        apart(sp)
                        load_ctxT0(p + 1)
                    load_ctx(p, g)

            with sp.Fori(0, NT // 2 - 1) as i:
                load_a(2 * i + 1, 0, True)
                load_a(2 * i + 2, 1, True)
            load_a(NT - 1, 0, False)

            sp.wait_ge(e_done, STEPS * NT)
            sp.wait_ge(n_stored, 16 * NT)
            sp.dma_start(tok[:, 0:NT - 1, :], n_dram[0:NT - 1].rearrange("t p n -> p t n")).then_inc(n_in, 16)
            sp.wait_ge(s_stored, 16 * NT)
            sp.wait_ge(pv_done, G * NT - 2)
            for i in range(2):
                h4 = slice(4 * i, 4 * i + 4)
                sp.dma_start(xo[:, h4, :], s_dram[h4].rearrange("t p n -> p t n")).then_inc(s_in[i], 16)
            for i in range(3):
                sp.dma_start(wqkv_sb[:, i], wqkv[0, :, i]).then_inc(wqkv_in[i], 16)
            sp.wait_ge(w_used, 2 * WT)

            def load_w2(h, i):
                sp.dma_start(w_buf[:, i % 2, :], pick(w_v[i // 4], 4 * h + i % 4)).then_inc(w2_in[i % 2], 16)

            load_w2(0, 0)
            load_w2(0, 1)
            sp.wait_ge(relu_done, NT)
            sp.wait_ge(xs_ready, NT)
            sp.dma_start(wo_sb[:, :, :], wo.rearrange("(c p) n -> p c n", p=P)).then_inc(wo_in, 16)

            def refill(h, last):
                for i in range(8):
                    if i == 1 and not last:
                        sp.wait_ge(q_done, 2 * h + 2)
                        sp.dma_start(wqkv_sb[:, 0], wqkv[bass.ds(h + 1, 1), :, 0].rearrange("a p c f -> p (a c) f"))\
                          .then_inc(wqkv_in[0], 16)
                    if i == 4 and not last:
                        sp.wait_ge(k_done, 2 * h + 2)
                        sp.dma_start(wqkv_sb[:, 1], wqkv[bass.ds(h + 1, 1), :, 1].rearrange("a p c f -> p (a c) f"))\
                          .then_inc(wqkv_in[1], 16)
                    if i == 7 and not last:
                        sp.wait_ge(v_done, 2 * h + 2)
                        sp.dma_start(wqkv_sb[:, 2], wqkv[bass.ds(h + 1, 1), :, 2].rearrange("a p c f -> p (a c) f"))\
                          .then_inc(wqkv_in[2], 16)
                    sp.wait_ge(t_ready, 8 * h + i + 1)
                    apart(sp)
                    if i < 6:
                        load_w2(h, i + 2)
                    elif not last:
                        load_w2(h + 1, i - 6)
                    sp.dma_start(pick(t_v[i // 4], 4 * h + i % 4), t_out[:, i % 2, :]).then_inc(t_stored[i % 2], 16)

            with sp.Fori(0, H - 1) as h:
                refill(h, False)
            refill(H - 1, True)

            for i in range(2):
                sp.wait_ge(t_stored[i], 16 * WT)
            sp.wait_ge(t_counted, 2 * WT)
            sp.wait_ge(x3_tr, 2 * NT)
            for k in range(4):
                sp.dma_start(t_buf[:, k, :].rearrange("p (c f) -> p c f", f=P), t1_v[k]).then_inc(t_in[k], 16)
            with sp.Fori(1, HC // 4) as i:
                for k in range(4):
                    sp.wait_ge(h_done, 8 * i + (2 * k - 6))
                    sp.dma_start(t_buf[:, k, :].rearrange("p (c f) -> p c f", f=P),
                                 t1_v[bass.ds(4 * i + k, 1)].rearrange("a p c f -> p (a c) f")).then_inc(t_in[k], 16)
            for k in range(4):
                sp.wait_ge(h_done, 2 * HC - 6 + 2 * k)
                sp.dma_start(t_buf[:, k, :], t2_v[k]).then_inc(t_in[k], 16)
            sp.wait_ge(h_ready, 2 * HC + 2)
            sp.dma_start(b2_bc[:, :], b2.partition_broadcast(P)).then_inc(b2_in, 16)
            with sp.Fori(1, HC // 4) as i:
                for k in range(4):
                    sp.wait_ge(t2_used, 4 * i + (k - 3))
                    sp.dma_start(t_buf[:, k, :], t2_v[bass.ds(4 * i + k, 1)].rearrange("a p n -> p (a n)"))\
                      .then_inc(t_in[k], 16)
            for k in range(4):
                if k < 3:
                    sp.wait_ge(t2_used, HC + k - 3)
                else:
                    sp.wait_ge(y_done, 8)
                sp.dma_start(t_buf[:, k, :], t2_v[k]).then_inc(t_in[k], 16)
            with sp.Fori(1, HC // 4) as i:
                for k in range(4):
                    sp.wait_ge(t2_used, 4 * i + (HC - 1 + k - 3))
                    sp.dma_start(t_buf[:, k, :], t2_v[bass.ds(4 * i + k, 1)].rearrange("a p n -> p (a n)"))\
                      .then_inc(t_in[k], 16)
            for t in range(NT):
                by_pool = sum(u in POOL_TILES for u in range(t + 1))
                if t in POOL_TILES:
                    sp.wait_ge(pool_ready, by_pool)
                else:
                    sp.wait_ge(q_ready, t + 1 - by_pool)
                sp.dma_start(out_v[:, t, :], xo[:, t, :]).then_inc(out_stored, 16)
            sp.wait_ge(out_stored, 16 * NT)

        @block.gpsimd
        def _(pool):
            for b in range(2):
                pool.memset(conv_bd[C * b:C * b + C, C * (1 - b):C * (1 - b) + C], 0.0).then_inc(tz, 1)
            pool.wait_ge(wmax_ready, 2)
            pool.partition_all_reduce(thr[:, 0, :], thr[:, 1, :], P, RED.max).then_inc(wmax_all, 1)
            pool.wait_ge(bmax_ready, 1)
            pool.partition_all_reduce(al[:, 0:1], al[:, 1:2], P, RED.max).then_inc(bmax_all, 1)
            pool.wait_ge(y_max, 1)
            pool.partition_all_reduce(ym[:, 17:18], ym[:, 16:17], P, RED.max).then_inc(y_all, 1)
            for t in POOL_TILES:
                pool.wait_ge(clip_ready, t + 1)
                pool.tensor_tensor(xo[:, t, :], xo[:, t, :], y[:, t, :], ALU.add).then_inc(pool_ready, 1)

        @block.scalar
        def _(act):
            A = act.activation

            def sqrt(n, view=slice(0, NT)):
                act.wait_ge(var_ready, n)
                A(rs[:, 1, view], rs[:, 0, view], ACT.Sqrt).then_inc(root_ready, 1)

            def load_w(p, i):
                act.dma_start(wa_buf[:, i % 4, :], pick(w_v[i // 4], 4 * p + i % 4)).then_inc(w_in[i % 4], 16)

            act.sem_inc(n_stored, 16)
            sqrt(1, slice(0, 1))
            for u in (0, 2):
                act.wait_ge(tr_ready, u + 1)
                c = slice(3 * u, min(3 * u + 3, NC))
                n = (c.stop - c.start) * P
                A(flat(x1T[:, c, :]), bank(5 + u, n), ACT.Copy).then_inc(tr_free[u], 1)

            def tile_a(p, par, nxt, start=False):
                for s in range(STEPS):
                    if s >= 2:
                        act.wait_ge(e_done, STEPS * p + (s - 1))
                    for k in range(4) if s == 0 else (0, 2):
                        u = 4 * s + k
                        n = BANK if s < STEPS - 1 else 4 * TAIL
                        act.wait_ge(tr_ready, UNITS * p + (TB + u + 1))
                        A(ctxT[:, s % 2, k, 0:n], bank(5 + u % TB, n), ACT.Copy).then_inc(tr_free[u % TB], 1)
                    if 1 <= s <= 4 and not start:
                        act.wait_ge(w_used, 8 * p + (s - 4))
                        load_w(p, s - 1)
                    if s == 4 and nxt is not None:
                        act.wait_ge(var_ready, p + 2)
                        A(rs[:, 1, 0:1], rs[:, 0, 0:1], ACT.Sqrt).then_inc(root_ready, 1)
                    if s == 6 and nxt is not None:
                        act.wait_ge(s_ready, p + 2)
                        act.dma_start(s_dram[bass.ds(p + 1, 1)].rearrange("a p n -> p (a n)"), x_t[:, :])\
                           .then_inc(s_stored, 16)
                if nxt is not None:
                    act.wait_ge(tr_ready, UNITS * p + (TB + U_X1 + 1))
                    A(flat(x1T[:, 0:4, :]), bank(5 + U_X1 % TB), ACT.Copy).then_inc(tr_free[U_X1 % TB], 1)
                act.wait_ge(nmax_ready, p + 1)
                A(prob[:, 0:BANK], bank(par), ACT.Exp, bias=nmx[:, 0:1], accum_out=zs[:, 0:1]).then_inc(exp_done, 1)
                A(prob[:, BANK:M], ps[:, 2 * BANK:BANK + M], ACT.Exp, bias=nmx[:, 0:1], accum_out=zs[:, 1:2])\
                    .then_inc(exp_done, 1)
                if nxt:
                    act.wait_ge(s_stored, 16 * p + 32)
                    act.dma_start(x_t[:, :], x_v[bass.ds(p + 2, 1)].rearrange("a p n -> p (a n)")).then_inc(x_in, 16)
                for i in range(4):
                    act.wait_ge(w_used, 8 * p + (i + 1))
                    load_w(p, i + 4)
                act.wait_ge(xr_done, p + 1)
                A(xr_sb[:, 0:BANK], bank(2), ACT.Copy).then_inc(xr_act, 1)

            tile_a(0, 0, True, True)
            with act.Fori(0, NT // 2 - 2) as i:
                tile_a(2 * i + 1, 1, True)
                tile_a(2 * i + 2, 0, True)
            tile_a(NT - 3, 1, True)
            tile_a(NT - 2, 0, False)
            tile_a(NT - 1, 1, None)

            act.wait_ge(lam_ready, 1)
            A(lam_sb[:, 4 * D + 2:4 * D + 4], lam_sb[:, 4 * D:4 * D + 2], ACT.Exp).then_inc(lam_exp, 1)
            sqrt(NT + 1, slice(0, 1))
            act.wait_ge(bn_ready, 1)

            for hb in range(2):
                if hb == 0:
                    act.wait_ge(n_in, 16)
                for t in range(4 * hb, 4 * hb + 4):
                    src = tok[:, t, :] if t < NT - 1 else x1s[:, 1, :]
                    A(tok[:, t, :], src, ACT.Relu, bias=bnm[:, 7:8], scale=bnm[:, 6:7]).then_inc(relu_done, 1)
                act.wait_ge(var_ready, NT + 2 + hb)
                A(rs[:, 1, 0:4], rs[:, 0, 0:4], ACT.Sqrt).then_inc(root_ready, 1)
                for t in range(4 * hb, 4 * hb + 4):
                    act.wait_ge(x2_tr, 2 * t + 1)
                    A(x2T[:, 0:4, P * t:P * t + P], bank(4 + 2 * (t % 2)).rearrange("p (c n) -> p c n", n=P), ACT.Copy)\
                        .then_inc(x2_act, 1)

            def count(h, i):
                act.wait_ge(t_counted, 8 * h + i)
                act.wait_ge(t_ready, 8 * h + i + 1)
                A(o_cnt[:, :], t_out[:, i % 2, :], ACT.Square, accum_out=wacc[:, i // 4, 1, i % 4:i % 4 + 1])\
                    .then_inc(t_counted, 1)

            def finish(h):
                act.wait_ge(at_done, 2 * h - 1)
                A(flat(aT[:, 0:4, :]), bank(6), ACT.Copy).then_inc(a_out[0], 1)
                act.wait_ge(o_done, h)
                A(flat(o_sq[:, :, :]), ps[:, 4 * BANK:6 * BANK], ACT.Square).then_inc(sq_done, 1)
                act.wait_ge(var_ready, h + (NT + 3))
                A(rs[:, 1, :], rs[:, 0, :], ACT.Sqrt).then_inc(root_ready, 1)

            def put_oT(h):
                act.wait_ge(ot_done, 2 * h - 1)
                apart(act)
                A(pick(oT, h - 1)[:, 0:BANK], bank(6), ACT.Copy, scale=cols[:, 3:4]).then_inc(oT_out[0], 1)

            def exps(h):
                act.wait_ge(sh_ready, h + 1)
                A(flat4(sm[:, :, :, :]), flat4(sm[:, :, :, :]), ACT.Exp, scale=float(D) ** -0.5).then_inc(p_ready, 1)

            def head(h, first):
                count(h, 0)
                count(h, 1)
                act.wait_ge(q_done, 2 * h + 1)
                A(qT[:, 0:BANK], bank(0), ACT.Copy).then_inc(q_out[0], 1)
                for i in range(2, 4):
                    count(h, i)
                act.wait_ge(k_done, 2 * h + 1)
                A(kT[:, 0:BANK], bank(2), ACT.Copy).then_inc(k_out[0], 1)
                count(h, 4)
                if not first:
                    finish(h)
                count(h, 5)
                act.wait_ge(v_done, 2 * h + 1)
                A(flat(v_sb[:, 0:4, :]), bank(0), ACT.Copy).then_inc(v_out[0], 1)
                if not first:
                    put_oT(h)
                count(h, 6)
                count(h, 7)
                exps(h)

            head(0, True)
            with act.Fori(1, H) as h:
                head(h, False)
            finish(H)
            put_oT(H)

            for t in range(NT):
                act.wait_ge(var_ready, NT + H + 4 + t)
                A(rs[:, 1, 0:1], rs[:, 0, 0:1], ACT.Sqrt).then_inc(root_ready, 1)
                for j in range(2):
                    act.wait_ge(x3_tr, 2 * t + j + 1)
                    A(x3h[:, 4 * j:4 * j + 4, P * t:P * t + P], bank(4 + 2 * (t % 2) + j).rearrange("p (c n) -> p c n", n=P),
                      ACT.Copy).then_inc(x3_hi, 1)
            act.wait_ge(al_ready, 1)
            act.sem_inc(g_ready, 8)

            with act.Fori(0, HC // 4) as i:
                for k in range(4):
                    for j in range(2):
                        n = 2 * k + j
                        act.wait_ge(h_done, 8 * i + (n + 1))
                        act.wait_ge(h_ready, 8 * i + (n + 1))
                        apart(act)
                        A(g_buf[:, j, :], bank(n), ACT.Gelu, bias=b1_sb[:, bass.ds(4 * i + k, 1)],
                          scale=al[:, 2:3]).then_inc(g_ready, 1)
            act.wait_ge(d_vec, 2)
            def rounded(t):
                A(y[:, t, :], y[:, t, :], ACT.Copy, scale=ym[:, 20:21], bias=ROUND).then_inc(z_ready, 1)

            rounded(0)
            for t in range(NT):
                if t < NT - 1:
                    rounded(t + 1)
                if t in POOL_TILES:
                    continue
                act.wait_ge(clip_ready, t + 1)
                A(y[:, t, :], y[:, t, :], ACT.Copy, bias=-ROUND).then_inc(whole_ready, 1)

        @block.tensor
        def _(pe):
            mm = pe.matmul

            pe.wait_ge(cst_in, 16)
            pe.wait_ge(x1s_ready, 1)
            for u in range(TB):
                for c in range(3 * u, min(3 * u + 3, NC)):
                    ins = pe.transpose(bank(5 + u)[:, (c - 3 * u) * P:(c - 3 * u + 1) * P], x1s[:, 0, c * P:c * P + P], ident)
                ins.then_inc(tr_ready, 1)

            def energies0(p, par, chunks):
                for c in chunks:
                    for b in range(2):
                        ins = mm(bank(par)[C * b:C * b + C, :], x1T[:, c, C * b:C * b + C], ctxT0[:, b, c, :],
                                 start=(c == 0), stop=(c == NC - 1))
                if c == NC - 1:
                    ins.then_inc(e0_done, 1)

            for k in range(TB):
                pe.wait_ge(tr_free[k], 1)
            for k in range(4):
                pe.wait_ge(first_T0[k], 32)
                energies0(0, 0, range(2 * k, 2 * k + 2))

            def free(p, u):
                pe.wait_ge(tr_free[u % TB], USES * p + (1 + u // TB))

            def copied(p, u):
                pe.wait_ge(tr_free[u % TB], USES * p + (2 + u // TB))

            def transposes(p, s):
                g, j = 1 + s // 4, s % 4
                if isinstance(p, int) and p == 0 and g < 3:
                    pe.wait_ge(first_g[g - 1][j], 32)
                elif j == 0:
                    pe.wait_ge(ctx_in[g], 32 * p + (0 if g < 3 else 32))
                for k in range(4):
                    u = 4 * s + k
                    free(p, u)
                    t = bank(5 + u % TB)
                    b = k % 2
                    for i in range(4):
                        if s < STEPS - 1:
                            c = 2 * j + k // 2
                            ins = pe.transpose(t[:, i * P:i * P + P], ctx_sb[:, b, 4 * g + i, c * P:c * P + P], ident)
                        else:
                            c = 4 * (k // 2) + i
                            ins = pe.transpose(t[:, i * TAIL:i * TAIL + TAIL],
                                               ctx_sb[0:TAIL, b, MT - 1, c * P:c * P + P], ident[0:TAIL, 0:TAIL])
                    ins.then_inc(tr_ready, 1)

            def energies(p, s):
                g, j = 1 + s // 4, s % 4
                for k in range(4):
                    copied(p, 4 * s + k)
                if s < STEPS - 1:
                    for i in range(2):
                        c = 2 * j + i
                        for b in range(2):
                            ins = mm(bank(1 + g)[C * b:C * b + C, :], x1T[:, c, C * b:C * b + C],
                                     ctxT[:, s % 2, 2 * i + b, :], start=(c == 0), stop=(c == NC - 1))
                else:
                    for c in range(NC):
                        for b in range(2):
                            ins = mm(bank(1 + g)[C * b:C * b + C, 0:TAIL], x1T[:, c, C * b:C * b + C],
                                     ctxT[:, s % 2, 2 * (c // 4) + b, (c % 4) * TAIL:(c % 4 + 1) * TAIL],
                                     start=(c == 0), stop=(c == NC - 1))
                ins.then_inc(e_done, 1)

            def tile_a(p, par, nxt):
                for s in range(STEPS + 1):
                    if s < STEPS:
                        transposes(p, s)
                    if s > 0:
                        energies(p, s - 1)
                u_at = U_AT if nxt else U_X1
                if nxt:
                    pe.wait_ge(x1s_ready, p + 2)
                    for k in range(2):
                        free(p, U_X1 + k)
                        for j in range(4):
                            c = 4 * k + j
                            ins = pe.transpose(bank(5 + (U_X1 + k) % TB)[:, j * P:j * P + P],
                                               x1s[:, 1 - par, c * P:c * P + P], ident)
                        ins.then_inc(tr_ready, 1)
                    for k in range(2):
                        copied(p, U_X1 + k)
                    pe.wait_ge(ctxT0_in, 32 * p + 32)
                    energies0(p, 1 - par, range(6))
                order = ORDER if nxt else LAST_ORDER
                pe.wait_ge(attn_ready, p + 1)
                for n, g in enumerate(order):
                    if n == TB and nxt:
                        energies0(p, 1 - par, range(6, NC))
                    free(p, u_at + n)
                    for i in range(4 if g < 3 else 1):
                        m0 = (4 * g + i) * P
                        w = min(P, M - m0)
                        ins = pe.transpose(bank(5 + (u_at + n) % TB)[0:w, i * P:i * P + P], prob[:, m0:m0 + w], ident)
                    ins.then_inc(tr_ready, 1)
                for n, g in enumerate(order):
                    copied(p, u_at + n)
                    if g == 0:
                        pe.wait_ge(ctx_in[0], 32 * p + 32)
                    mts = range(4 * g, 4 * g + 4) if g < 3 else [MT - 1]
                    first, last = 4 * order[0], 4 * order[-1] + 3
                    parts = [(mt, hf) for hf in range(2) for mt in mts] if n == G - 1 else \
                            [(mt, hf) for mt in mts for hf in range(2)]
                    for mt, hf in parts:
                        w = P if mt < MT - 1 else TAIL
                        for b in range(2):
                            ins = mm(bank(2 + hf)[C * b:C * b + C, :], attnT[0:w, mt, C * b:C * b + C],
                                     ctx_sb[0:w, b, mt, hf * BANK:hf * BANK + BANK], start=(mt == first), stop=(mt == last))
                        if mt == last and hf == 0:
                            ins.then_inc(xr_done, 1)
                    ins.then_inc(pv_done, 1)
                if isinstance(p, int) and p == 0:
                    pe.wait_ge(small_in, 16 * 11)
                    pe.wait_ge(tz, 2)
                for hf, s in enumerate((xr_act, xr_dve)):
                    pe.wait_ge(s, p + 1)
                    mm(bank(4 if hf == 0 else par), conv_bd[:, :], xr_sb[:, hf * BANK:hf * BANK + BANK], start=True, stop=True)\
                        .then_inc(cv_done, 1)

            tile_a(0, 0, True)
            with pe.Fori(0, NT // 2 - 1) as i:
                tile_a(2 * i + 1, 1, True)
                tile_a(2 * i + 2, 0, True)
            tile_a(NT - 1, 1, False)

            pe.wait_ge(bn_part, 1)
            mm(bank(0, 2), cst[:, C_PAIR:C_PAIR + P], bnm[:, 0:2], start=True, stop=True).then_inc(bn_avg, 1)

            def put_x2T(t):
                pe.wait_ge(xs_ready, t + 1)
                for j in range(2):
                    if t >= 2:
                        pe.wait_ge(x2_act if j == 0 else x2_dve, t - 1)
                    for i in range(4):
                        c = 4 * j + i
                        ins = pe.transpose(bank(4 + 2 * (t % 2) + j)[:, i * P:i * P + P], xs[:, t % 2, c * P:c * P + P], ident)
                    ins.then_inc(x2_tr, 1)

            for t in range(4):
                put_x2T(t)

            def proj_T(h, w, w_sem, b0, done, frees, halves=(0, 1), first=False):
                pe.wait_ge(w_sem, 16 * h + 16)
                for s, n in frees:
                    pe.wait_ge(s, n)
                for hf in halves:
                    if first:
                        pe.wait_ge(x2_act, 4 * hf + 4)
                        pe.wait_ge(x2_dve, 4 * hf + 4)
                    for c in range(NC):
                        ins = mm(bank(b0 + hf), wqkv_sb[:, w, c, :], x2T[:, c, hf * BANK:hf * BANK + BANK],
                                 start=(c == 0), stop=(c == NC - 1))
                    ins.then_inc(done, 1)

            def turn(h):
                pe.wait_ge(a_ready, 2 * h)
                for j in range(2):
                    for i in range(4):
                        ins = pe.transpose(bank(6 + j)[:, i * P:i * P + P], a_bd[:, 4 * j + i, :], ident)
                    ins.then_inc(at_done, 1)

            def weigh(h):
                for j in range(2):
                    pe.wait_ge(a_out[j], h)
                    pe.wait_ge(v_out[j], h)
                    for i in range(4):
                        t = 4 * j + i
                        ins = mm(bank(4 + j)[:, i * P:i * P + P], aT[:, t, :], v_sb[:, t, :], start=True, stop=True)
                ins.then_inc(o_done, 1)

            def put_oT(h):
                pe.wait_ge(on_ready, h)
                for j in range(2):
                    for i in range(4):
                        ins = pe.transpose(bank(6 + j)[:, i * P:i * P + P], o_n[:, 4 * j + i, :], ident)
                    ins.then_inc(ot_done, 1)

            def head(h, first):
                if first:
                    for hf in range(2):
                        proj_T(h, 0, wqkv_in[0], 0, q_done, [], (hf,), True)
                        proj_T(h, 1, wqkv_in[1], 2, k_done, [], (hf,), True)
                        if hf == 0:
                            for t in range(4, NT):
                                put_x2T(t)
                else:
                    proj_T(h, 0, wqkv_in[0], 0, q_done, [(v_out[0], h), (v_out[1], h)])
                    proj_T(h, 1, wqkv_in[1], 2, k_done, [(k_out[0], h), (k_out[1], h)])
                if not first:
                    turn(h)
                pe.wait_ge(wqkv_in[2], 16 * h + 16)
                for hf in range(2):
                    if hf == 1 and not first:
                        weigh(h)
                    pe.wait_ge(q_out[hf], h + 1)
                    for i in range(4):
                        t = 4 * hf + i
                        for c in range(NC):
                            ins = mm(bank(hf)[:, i * P:i * P + P], x2T[:, c, t * P:t * P + P], wqkv_sb[:, 2, c, :],
                                     start=(c == 0), stop=(c == NC - 1))
                    ins.then_inc(v_done, 1)
                if not first:
                    put_oT(h)
                for j in range(2):
                    pe.wait_ge(k_out[j], h + 1)
                apart(pe)
                for t in range(NT):
                    for b in range(2):
                        for u in range(2):
                            tk = slice(t * P + C * b, t * P + C * b + C)
                            ins = mm(bank(4 + u)[C * b:C * b + C, t * D:t * D + D], qT[D * u:D * u + D, tk],
                                     kT[D * u:D * u + D, tk], start=True, stop=True)
                ins.then_inc(s_done, 1)

            head(0, True)
            with pe.Fori(1, H) as h:
                head(h, False)
            def project(t, heads):
                for hf in range(2):
                    if t >= 2:
                        pe.wait_ge(x3_done, 2 * (t - 2) + hf + 1)
                    for c in heads:
                        ins = mm(bank(2 * (t % 2) + hf), oT[:, c, t * P:t * P + P], wo_sb[:, c, hf * BANK:hf * BANK + BANK],
                                 start=(c == 0), stop=(c == H - 1))
                    if c == H - 1:
                        ins.then_inc(pr_done, 1)

            pe.wait_ge(wo_in, 16)
            for j in range(2):
                pe.wait_ge(oT_out[j], H - 1)
                pe.wait_ge(v_out[j], H)
                pe.wait_ge(k_out[j], H)
            project(0, range(H - 1))
            project(1, range(H - 1))
            turn(H)
            weigh(H)
            put_oT(H)

            pe.wait_ge(tot_ready, 1)
            mm(bank(4, 4), cst[:, C_ONE:C_ONE + P], wtot[:, :], start=True, stop=True).then_inc(tot_sum, 1)
            pe.wait_ge(oT_out[0], H)
            pe.wait_ge(oT_out[1], H)
            for t in range(NT + 1):
                if t < NT:
                    project(t, [H - 1] if t < 2 else range(H))
                if t >= 1:
                    pe.wait_ge(xs_ready, NT + t)
                    for j in range(2):
                        if t >= 3:
                            pe.wait_ge(x3_lo, 2 * (t - 3) + j + 1)
                        for i in range(4):
                            c = 4 * j + i
                            ins = pe.transpose(bank(4 + 2 * ((t - 1) % 2) + j)[:, i * P:i * P + P],
                                               xs[:, (t - 1) % 2, c * P:c * P + P], ident)
                        ins.then_inc(x3_tr, 1)

            pe.wait_ge(x3_lo, 2 * NT)
            with pe.Fori(0, HC // 4) as i:
                for k in range(4):
                    pe.wait_ge(t_in[k], 16 * i + 16)
                    for j in range(2):
                        pe.wait_ge(g_ready, 8 * i + (2 * k + j + 1))
                    for c in range(NC):
                        for n, part in enumerate((x3h, x3l)):
                            for j in range(2):
                                ins = mm(bank(2 * k + j), t_buf[:, k, c * P:c * P + P], part[:, c, j * BANK:j * BANK + BANK],
                                         start=(c == 0 and n == 0), stop=(c == NC - 1 and n == 1))
                                if c == NC - 1 and n == 1:
                                    ins.then_inc(h_done, 1)

            def chunk(q, i, k, start, stop, tiles=range(4)):
                pe.wait_ge(t_in[k], 16 * (HC // 4) * (1 + q) + 16 * i + 16)
                hc = 4 * i + k
                for t in tiles:
                    for n, part in enumerate((h_hi, h_lo)):
                        lhs = part[:, bass.ds(hc, 1), (4 * q + t) * P:(4 * q + t + 1) * P].rearrange("p a n -> p (a n)")
                        for j in range(2):
                            b = 2 * t + j
                            if start and n == 0:
                                if q:
                                    pe.wait_ge(y_out, b + 1)
                            ins = mm(bank(b), lhs, t_buf[:, k, j * BANK:j * BANK + BANK],
                                     start=(start and n == 0), stop=(stop and n == 1))
                            if stop and n == 1:
                                ins.then_inc(y_done, 1)
                return ins

            pe.wait_ge(h_ready, 2 * HC + 2)
            for q in range(2):
                for k in range(4):
                    chunk(q, 0, k, k == 0, False).then_inc(t2_used, 1)
                with pe.Fori(1, HC // 4 - 1) as i:
                    for k in range(4):
                        chunk(q, i, k, False, False).then_inc(t2_used, 1)
                if q == 0:
                    for k in range(3):
                        chunk(q, HC // 4 - 1, k, False, False).then_inc(t2_used, 1)
                    chunk(q, HC // 4 - 1, 3, False, True)
                else:
                    for t in range(4):
                        for k in range(4):
                            chunk(q, HC // 4 - 1, k, False, k == 3, (t,))

        @block.vector
        def _(dve):
            V = dve

            def inverse_root(own, v, root, inv, tmp):
                own.done(V.reciprocal(inv, root))
                own.done(V.tensor_tensor(tmp, inv, inv, ALU.mult))
                own.done(V.tensor_tensor(tmp, tmp, v, ALU.mult))
                own.done(V.tensor_scalar(tmp, tmp, -0.5, 1.5, ALU.mult, ALU.add))
                own.done(V.tensor_tensor(inv, inv, tmp, ALU.mult))

            own = Own(V, vec)

            def stats(o):
                for j in range(2):
                    V.bn_stats(st[:, j, :], x_t[:, j * BANK:j * BANK + BANK]).then_inc(vec, 1)
                    o.n += 1
                V.wait_ge(vec, o.start + o.n)
                apart(V)
                o.done(V.bn_aggr(mv[:, 0, :], st[:, 0:2, :]))
                V.tensor_scalar(rs[:, 0, 0:1], mv[:, 0, 1:2], EPS, None, ALU.add).then_inc(var_ready, 1)

            def make_x1(o, n, par):
                V.wait_ge(root_ready, n)
                inverse_root(o, rs[:, 0, 0:1], rs[:, 1, 0:1], rs[:, 2, 0:1], t8[:, 0:1])
                if not (isinstance(n, int) and n == 1):
                    V.wait_ge(n_stored, 16 * (n - 1))
                V.tensor_scalar(x1s[:, par, :], x_t[:, :], mv[:, 0, 0:1], rs[:, 2, 0:1], ALU.subtract, ALU.mult)\
                    .then_inc(x1s_ready, 1)
                V.wait_ge(x1s_ready, n)
                V.tensor_tensor(x_t[:, :], x_t[:, :], x1s[:, par, :], ALU.add).then_inc(s_ready, 1)

            V.wait_ge(x_in, 16)
            stats(own)
            make_x1(own, 1, 0)
            V.wait_ge(tr_ready, 2)
            V.tensor_copy(flat(x1T[:, 3:6, :]), bank(6, 3 * P)).then_inc(tr_free[1], 1)
            VEC0 = own.n
            VEC_A = 26

            def largest(p, i):
                V.wait_ge(w_in[i % 4], 32 * p + 16 * (i // 4 + 1))
                V.tensor_reduce(wmx[:, i // 4, bass.ds(4 * p + i % 4, 1)], wa_buf[:, i % 4, :], AX.X, ALU.max,
                                apply_absolute_value=True).then_inc(w_used, 1)

            def tile_a(p, par, nxt, start=False):
                o = Own(V, vec, VEC_A * p + VEC0)
                for s in range(STEPS):
                    if s >= 2:
                        V.wait_ge(e_done, STEPS * p + (s - 1))
                    for k in () if s == 0 else (1, 3):
                        u = 4 * s + k
                        n = BANK if s < STEPS - 1 else 4 * TAIL
                        V.wait_ge(tr_ready, UNITS * p + (TB + u + 1))
                        V.tensor_copy(ctxT[:, s % 2, k, 0:n], bank(5 + u % TB, n)).then_inc(tr_free[u % TB], 1)
                    if s < 4 and not start:
                        largest(p - 1, s + 4)
                    if s == 1:
                        V.wait_ge(e0_done, p + 1)
                        o.done(V.tensor_reduce(mx4[:, 0:1], bank(par), AX.X, ALU.max))
                    if s == 2 and nxt:
                        V.wait_ge(x_in, 16 * p + 32)
                        stats(o)
                    if s == 5:
                        if nxt:
                            make_x1(o, p + 2, 1 - par)
                        V.wait_ge(e_done, STEPS * p + 4)
                        o.done(V.tensor_reduce(mx4[:, 1:2], bank(2), AX.X, ALU.max))
                V.wait_ge(e_done, STEPS * p + 8)
                o.done(V.tensor_reduce(mx4[:, 2:3], bank(3), AX.X, ALU.max))
                V.wait_ge(e_done, STEPS * p + STEPS)
                o.done(V.tensor_reduce(mx4[:, 3:4], bank(4, TAIL), AX.X, ALU.max))
                V.tensor_reduce(nmx[:, :], mx4[:, :], AX.X, ALU.max, negate=True).then_inc(nmax_ready, 1)
                if nxt:
                    V.wait_ge(tr_ready, UNITS * p + (TB + U_X1 + 2))
                    V.tensor_copy(flat(x1T[:, 4:8, :]), bank(5 + (U_X1 + 1) % TB)).then_inc(tr_free[(U_X1 + 1) % TB], 1)
                V.wait_ge(exp_done, 2 * p + 2)
                o.done(V.tensor_tensor(zs[:, 2:3], zs[:, 0:1], zs[:, 1:2], ALU.add))
                o.done(V.reciprocal(cs[:, 0:1], zs[:, 2:3]))
                V.tensor_scalar(prob[:, :], prob[:, :], cs[:, 0:1], None, ALU.mult).then_inc(attn_ready, 1)
                early = 2 if nxt and not start else 0
                for i in range(early):
                    largest(p, i)
                u_at = U_AT if nxt else U_X1
                for k, g in enumerate(ORDER if nxt else LAST_ORDER):
                    n, nt = (P, 4) if g < 3 else (TAIL, 1)
                    u = u_at + k
                    V.wait_ge(tr_ready, UNITS * p + (TB + u + 1))
                    t = bank(5 + u % TB)[0:n, 0:nt * P].rearrange("p (t c) -> p t c", c=C)
                    c = cs[0:n, 8 * k:8 * k + 2 * nt]
                    o.done(V.tensor_reduce(c, t, AX.X, ALU.add))
                    o.done(V.tensor_scalar(c, c, 1e-9, None, ALU.add))
                    o.done(V.reciprocal(c, c))
                    V.tensor_tensor(attnT[0:n, 4 * g:4 * g + nt, :].rearrange("p t (b c) -> p (t b) c", c=C), t,
                                    c.unsqueeze(2).broadcast_to([n, 2 * nt, C]), ALU.mult).then_inc(tr_free[u % TB], 1)
                for i in range(early, 4 if nxt else 8):
                    largest(p, i)
                if start:
                    V.wait_ge(small_in, 16 * 11)
                V.wait_ge(pv_done, G * p + G)
                V.tensor_copy(xr_sb[:, BANK:2 * BANK], bank(3)).then_inc(xr_dve, 1)
                for hf in range(2):
                    V.wait_ge(cv_done, 2 * p + (hf + 1))
                    tt = x1s[:, par, hf * BANK:hf * BANK + BANK]
                    V.scalar_tensor_tensor(tt, bank(4 if hf == 0 else par), cols[:, 0:1], tt, ALU.add, ALU.subtract)\
                        .then_inc(cv_free, 1)
                    V.wait_ge(cv_free, 2 * p + (hf + 1))
                    apart(V)
                    V.bn_stats(bn[:, bass.ds(p, 1), hf, :].rearrange("p a n -> p (a n)"), tt).then_inc(bn_st, 1)
                if nxt:
                    assert o.n == VEC_A, o.n
                return o

            tile_a(0, 0, True, True)
            with V.Fori(0, NT // 2 - 1) as i:
                tile_a(2 * i + 1, 1, True)
                tile_a(2 * i + 2, 0, True)
            o = tile_a(NT - 1, 1, False)
            own = Own(V, vec, VEC_A * (NT - 1) + VEC0 + o.n)

            V.wait_ge(bn_st, 2 * NT)
            V.bn_aggr(bnm[:, 0:2], bn[:, :, :, :].rearrange("p a b n -> p (a b n)")).then_inc(bn_part, 1)
            lam2 = lam_sb[:, 0:4 * D].rearrange("p (a b n) -> p a b n", a=2, b=2)
            own.done(V.tensor_tensor(lam2[:, :, 0, :], lam2[:, :, 0, :], lam2[:, :, 1, :], ALU.mult))
            V.tensor_reduce(lam_sb[:, 4 * D:4 * D + 2], lam2[:, :, 0, :], AX.X, ALU.add).then_inc(lam_ready, 1)
            V.wait_ge(w_used, 2 * WT)
            for i in range(2):
                V.tensor_reduce(thr[:, 1, i:i + 1], wmx[:, i, :], AX.X, ALU.max).then_inc(wmax_ready, 1)
            V.wait_ge(bn_avg, 1)
            own.done(V.tensor_copy(bnm[:, 2:4], bank(0, 2)))
            own.done(V.tensor_tensor(bnm[:, 4:5], bnm[:, 0:1], bnm[:, 2:3], ALU.subtract))
            own.done(V.tensor_tensor(bnm[:, 4:5], bnm[:, 4:5], bnm[:, 4:5], ALU.mult))
            V.scalar_tensor_tensor(rs[:, 0, 0:1], bnm[:, 4:5], EPS, bnm[:, 3:4], ALU.add, ALU.add).then_inc(var_ready, 1)
            V.wait_ge(root_ready, NT + 1)
            inverse_root(own, rs[:, 0, 0:1], rs[:, 1, 0:1], rs[:, 2, 0:1], t8[:, 0:1])
            own.done(V.tensor_tensor(bnm[:, 5:6], rs[:, 2, 0:1], cols[:, 1:2], ALU.mult))
            own.done(V.tensor_scalar(bnm[:, 6:7], bnm[:, 5:6], -1.0, None, ALU.mult))
            V.scalar_tensor_tensor(bnm[:, 7:8], bnm[:, 5:6], bnm[:, 2:3], cols[:, 2:3], ALU.mult, ALU.add).then_inc(bn_ready, 1)
            V.wait_ge(lam_exp, 1)
            L = 4 * D
            own.done(V.tensor_tensor(lam_sb[:, L + 4:L + 5], lam_sb[:, L + 2:L + 3], lam_sb[:, L + 3:L + 4], ALU.subtract))
            own.done(V.tensor_scalar(neg_lam[:, :], lam_sb[:, L + 4:L + 5], LAMBDA_INIT, -1.0, ALU.add, ALU.mult))
            own.done(V.tensor_scalar(cols[:, 3:4], cols[:, 3:4], 1.0 - LAMBDA_INIT, None, ALU.mult))
            V.wait_ge(wmax_all, 1)
            own.done(V.tensor_scalar(thr[:, 1, :], thr[:, 0, :], 0.05, None, ALU.mult))
            own.done(V.tensor_scalar(thr[:, 2, :], thr[:, 1, :], -1.0, None, ALU.mult))
            own.done(V.memset(wtot[:, :], 0.0))
            own.done(V.memset(a_bd[:, :, :], 0.0))
            V.tensor_reduce(al[:, 1:2], b1_sb[:, :], AX.X, ALU.max, apply_absolute_value=True).then_inc(bmax_ready, 1)
            for hb in range(2):
                V.wait_ge(s_in[hb], 16)
                for k in range(4):
                    t = 4 * hb + k
                    V.wait_ge(relu_done, t + 1)
                    own.done(V.tensor_tensor(xo[:, t, :], xo[:, t, :], tok[:, t, :], ALU.add))
                    for j in range(2):
                        V.bn_stats(st[:, 2 * k + j, :], xo[:, t, j * BANK:j * BANK + BANK]).then_inc(vec, 1)
                        own.n += 1
                for k in range(4):
                    if k == 0:
                        V.wait_ge(vec, own.start + own.n)
                    V.bn_aggr(mv[:, k, :], st[:, 2 * k:2 * k + 2, :]).then_inc(vec, 1)
                    own.n += 1
                V.wait_ge(vec, own.start + own.n)
                V.tensor_scalar(rs[:, 0, 0:4], mv[:, 0:4, 1], EPS, None, ALU.add).then_inc(var_ready, 1)
                V.wait_ge(root_ready, NT + 2 + hb)
                inverse_root(own, rs[:, 0, 0:4], rs[:, 1, 0:4], rs[:, 2, 0:4], t8[:, 0:4])
                for t in range(4 * hb, 4 * hb + 5):
                    if t < 4 * hb + 4:
                        if t >= 2:
                            V.wait_ge(x2_tr, 2 * t - 2)
                        k = t % 4
                        V.tensor_scalar(xs[:, t % 2, :], xo[:, t, :], mv[:, k, 0:1], rs[:, 2, k:k + 1],
                                        ALU.subtract, ALU.mult).then_inc(xs_ready, 1)
                    if t >= 4 * hb + 1:
                        V.wait_ge(x2_tr, 2 * t)
                        V.tensor_copy(x2T[:, 4:8, P * (t - 1):P * t],
                                      bank(5 + 2 * ((t - 1) % 2)).rearrange("p (c n) -> p c n", n=P)).then_inc(x2_dve, 1)

            VEC2 = own.start + own.n

            def ternary(o, h, i):
                m = i // 4
                V.wait_ge(w2_in[i % 2], 64 * h + 16 * (i // 2 + 1))
                t = t_out[:, i % 2, :]
                if i >= 2:
                    V.wait_ge(t_stored[i % 2], 64 * h + 16 * (i // 2))
                    V.wait_ge(t_counted, 8 * h + (i - 1))
                else:
                    V.wait_ge(t_stored[i % 2], 64 * h + 0)
                    V.wait_ge(t_counted, 8 * h + 0)
                o.done(V.tensor_scalar(t, w_buf[:, i % 2, :], thr[:, 2, m:m + 1], None, ALU.is_lt))
                o.done(V.scalar_tensor_tensor(t, w_buf[:, i % 2, :], thr[:, 1, m:m + 1], t, ALU.is_gt, ALU.subtract))
                V.wait_ge(t_ready, 8 * h + i)
                V.scalar_tensor_tensor(w_junk[:, :], w_buf[:, i % 2, :], 1.0, t, ALU.mult, ALU.mult,
                                       accum_out=wacc[:, m, 0, i % 4:i % 4 + 1]).then_inc(t_ready, 1)

            def turned(h):
                V.wait_ge(at_done, 2 * h)
                V.tensor_copy(flat(aT[:, 4:8, :]), bank(7)).then_inc(a_out[1], 1)

            def finish(o, h):
                V.wait_ge(sq_done, h)
                o.done(V.tensor_reduce(t8[:, :], o_sq[:, :, :], AX.X, ALU.add))
                V.tensor_scalar(rs[:, 0, :], t8[:, :], 1.0 / P, EPS, ALU.mult, ALU.add).then_inc(var_ready, 1)
                V.wait_ge(root_ready, h + (NT + 3))
                inverse_root(o, rs[:, 0, :], rs[:, 1, :], rs[:, 2, :], t8[:, :])
                V.tensor_tensor(o_n[:, :, :], ps[:, 4 * BANK:6 * BANK].rearrange("p (t n) -> p t n", n=P),
                                rs[:, 2, :].unsqueeze(2).broadcast_to([P, NT, P]), ALU.mult).then_inc(on_ready, 1)

            def put_oT(h):
                V.wait_ge(ot_done, 2 * h)
                V.tensor_scalar(pick(oT, h - 1)[:, BANK:2 * BANK], bank(7), cols[:, 3:4], None, ALU.mult)\
                    .then_inc(oT_out[1], 1)

            def softmax(o, h, first):
                V.wait_ge(s_done, h + 1)
                if not first:
                    V.wait_ge(at_done, 2 * h)
                s3 = sm[:, :, :, :].rearrange("p u t s -> p (u t) s")
                wide = lambda a: a.unsqueeze(2).broadcast_to([P, 2 * NT, D])
                mask = cst[:, C_MASK:C_MASK + D].unsqueeze(1).broadcast_to([P, 2 * NT, D])
                o.done(V.tensor_tensor(s3, ps[:, 4 * BANK:6 * BANK].rearrange("p (a s) -> p a s", s=D), mask, ALU.add))
                o.done(V.tensor_reduce(sx[:, 0, :], s3, AX.X, ALU.max))
                V.tensor_tensor(s3, s3, wide(sx[:, 0, :]), ALU.subtract).then_inc(sh_ready, 1)
                V.wait_ge(p_ready, h + 1)
                o.done(V.tensor_reduce(sx[:, 1, :], s3, AX.X, ALU.add))
                o.done(V.reciprocal(sx[:, 2, :], sx[:, 1, :]))
                o.done(V.tensor_scalar(sx[:, 2, NT:2 * NT], sx[:, 2, NT:2 * NT], neg_lam[:, 0:1], None, ALU.mult))
                o.done(V.tensor_tensor(s3, s3, wide(sx[:, 2, :]), ALU.mult))
                for b in range(2):
                    r = slice(C * b, C * b + C)
                    V.tensor_tensor(a_bd[r, :, C * b:C * b + C], sm[r, 0], sm[r, 1], ALU.add).then_inc(a_ready, 1)

            def head(h, first):
                o = Own(V, vec, VEC2 if first else VEC_HF * (h - 1) + (VEC2 + VEC_H))
                ternary(o, h, 0)
                ternary(o, h, 1)
                V.wait_ge(q_done, 2 * h + 2)
                V.tensor_copy(qT[:, BANK:2 * BANK], bank(1)).then_inc(q_out[1], 1)
                for i in range(2, 5):
                    ternary(o, h, i)
                V.wait_ge(k_done, 2 * h + 2)
                V.tensor_copy(kT[:, BANK:2 * BANK], bank(3)).then_inc(k_out[1], 1)
                if not first:
                    turned(h)
                ternary(o, h, 5)
                ternary(o, h, 6)
                if not first:
                    finish(o, h)
                V.wait_ge(v_done, 2 * h + 2)
                V.tensor_copy(flat(v_sb[:, 4:8, :]), bank(1)).then_inc(v_out[1], 1)
                if not first:
                    put_oT(h)
                ternary(o, h, 7)
                softmax(o, h, first)
                V.wait_ge(t_counted, 8 * h + 8)
                V.wait_ge(t_ready, 8 * h + 8)
                o.done(V.tensor_reduce(t8[:, 0:4], wacc[:, :, :, :].rearrange("p m k i -> p (m k) i"), AX.X, ALU.add))
                o.done(V.tensor_tensor(wtot[:, :], wtot[:, :], t8[:, 0:4], ALU.add))
                return o.n

            VEC_H = 16 + 6 + 2
            VEC_HF = VEC_H + 6
            assert head(0, True) == VEC_H
            with V.Fori(1, H) as h:
                assert head(h, False) == VEC_HF
            own = Own(V, vec, VEC2 + VEC_H + VEC_HF * (H - 1))
            V.sem_inc(tot_ready, 1)
            turned(H)
            finish(own, H)
            put_oT(H)

            V.wait_ge(tot_sum, 1)
            own.done(V.tensor_copy(wtot[:, :], bank(4, 4)))
            own.done(V.tensor_scalar(ym[:, 0:4], wtot[:, :], 1.0, None, ALU.max))
            own.done(V.reciprocal(ym[:, 4:8], ym[:, 0:4]))
            own.done(V.tensor_tensor(ym[:, 8:9], wtot[:, 0:1], ym[:, 5:6], ALU.mult))
            own.done(V.tensor_tensor(ym[:, 9:10], wtot[:, 2:3], ym[:, 7:8], ALU.mult))
            V.wait_ge(bmax_all, 1)
            own.done(V.tensor_scalar(al[:, 4:5], ym[:, 8:9], float(N), al[:, 0:1], ALU.mult, ALU.add))
            own.done(V.tensor_scalar(al[:, 4:5], al[:, 4:5], 1e-20, 1.0 / H_RANGE, ALU.max, ALU.mult))
            own.done(V.reciprocal(al[:, 3:4], al[:, 4:5]))
            own.done(V.tensor_tensor(al[:, 5:6], al[:, 4:5], ym[:, 9:10], ALU.mult))
            V.tensor_scalar(al[:, 2:3], ym[:, 8:9], 1.0 / X_SCALE, None, ALU.mult).then_inc(al_ready, 1)

            for t in range(NT + 1):
                if t < NT:
                    for hf in range(2):
                        V.wait_ge(pr_done, 2 * t + hf + 1)
                        xh = xo[:, t, hf * BANK:hf * BANK + BANK]
                        V.tensor_tensor(xh, bank(2 * (t % 2) + hf), xh, ALU.add).then_inc(x3_done, 1)
                        V.wait_ge(x3_done, 2 * t + hf + 1)
                        own.done(V.bn_stats(st[:, hf, :], xh))
                    own.done(V.bn_aggr(mv[:, 0, :], st[:, 0:2, :]))
                    V.tensor_scalar(rs[:, 0, 0:1], mv[:, 0, 1:2], EPS, None, ALU.add).then_inc(var_ready, 1)
                    V.wait_ge(root_ready, NT + H + 4 + t)
                    inverse_root(own, rs[:, 0, 0:1], rs[:, 1, 0:1], rs[:, 2, 0:1], t8[:, 0:1])
                    own.done(V.tensor_scalar(rs[:, 2, 1:2], rs[:, 2, 0:1], X_SCALE, None, ALU.mult))
                    if t >= 2:
                        V.wait_ge(x3_tr, 2 * (t - 1))
                    V.tensor_scalar(xs[:, t % 2, :], xo[:, t, :], mv[:, 0, 0:1], rs[:, 2, 1:2], ALU.subtract, ALU.mult)\
                        .then_inc(xs_ready, 1)
                if t >= 1:
                    for j in range(2):
                        V.wait_ge(x3_hi, 2 * (t - 1) + j + 1)
                        c = slice(4 * j, 4 * j + 4)
                        V.tensor_tensor(x3l[:, c, P * (t - 1):P * t],
                                        bank(4 + 2 * ((t - 1) % 2) + j).rearrange("p (c n) -> p c n", n=P),
                                        x3h[:, c, P * (t - 1):P * t], ALU.subtract).then_inc(x3_lo, 1)

            V.sem_inc(h_ready, 2)
            with V.Fori(0, HC // 4) as i:
                for k in range(4):
                    for j in range(2):
                        n = 2 * k + j
                        V.wait_ge(g_ready, 8 * i + (8 + n + 1))
                        c = slice(j * BANK, j * BANK + BANK)
                        hi, lo = pick(h_hi, 4 * i + k)[:, c], pick(h_lo, 4 * i + k)[:, c]
                        V.tensor_scalar(hi, g_buf[:, j, :], al[:, 3:4], None, ALU.mult).then_inc(h_high, 1)
                        V.wait_ge(h_high, 8 * i + (n + 1))
                        V.scalar_tensor_tensor(lo, g_buf[:, j, :], al[:, 3:4], hi, ALU.mult, ALU.subtract)\
                            .then_inc(h_ready, 1)

            V.wait_ge(b2_in, 16)
            for q in range(2):
                for b in range(8):
                    V.wait_ge(y_done, 8 * q + b + 1)
                    t, j = 4 * q + b // 2, b % 2
                    yh = y[:, t, j * BANK:j * BANK + BANK]
                    V.scalar_tensor_tensor(yh, bank(b), al[:, 5:6], b2_bc[:, j * BANK:j * BANK + BANK], ALU.mult, ALU.add)\
                        .then_inc(y_out, 1)
                    V.wait_ge(y_out, 8 * q + b + 1)
                    own.done(V.tensor_reduce(ym[:, 8 * q + b:8 * q + b + 1], yh, AX.X, ALU.max, apply_absolute_value=True))
            V.tensor_reduce(ym[:, 16:17], ym[:, 0:16], AX.X, ALU.max).then_inc(y_max, 1)

            V.wait_ge(y_all, 1)
            d = Own(V, d_vec)
            d.done(V.tensor_scalar(ym[:, 19:20], ym[:, 17:18], 1.0 / QMAX, 1e-8, ALU.mult, ALU.add))
            d.done(V.reciprocal(ym[:, 20:21], ym[:, 19:20]))
            def clip(t):
                V.wait_ge(z_ready, t + 1)
                if t in POOL_TILES:
                    own.done(V.tensor_scalar(y[:, t, :], y[:, t, :], -ROUND, QMAX, ALU.add, ALU.min))
                    V.tensor_scalar(y[:, t, :], y[:, t, :], -QMAX, ym[:, 19:20], ALU.max, ALU.mult).then_inc(clip_ready, 1)
                else:
                    V.tensor_scalar(y[:, t, :], y[:, t, :], ROUND + QMAX, ROUND - QMAX, ALU.min, ALU.max)\
                        .then_inc(clip_ready, 1)

            clip(0)
            clip(1)
            n = 0
            for t in range(NT):
                if t + 2 < NT:
                    clip(t + 2)
                if t not in POOL_TILES:
                    n += 1
                    V.wait_ge(whole_ready, n)
                    V.scalar_tensor_tensor(xo[:, t, :], y[:, t, :], ym[:, 19:20], xo[:, t, :], ALU.mult, ALU.add)\
                        .then_inc(q_ready, 1)


_INS = ("x", "ctx", "ctx0T", "conv_wT", "conv_b", "bn_gamma", "bn_beta", "wqkv", "wo", "lambdas", "g", "w1t", "b1", "w2t", "b2",
        "consts")


def kernel(x, ctx_2048, L0_xattn_conv_w, L0_xattn_conv_b, L0_xattn_bn_gamma, L0_xattn_bn_beta, L0_attn_Wq, L0_attn_Wk,
           L0_attn_Wv, L0_attn_Wo, L0_attn_lambda_q1, L0_attn_lambda_k1, L0_attn_lambda_q2, L0_attn_lambda_k2,
           L0_attn_g, L0_ffn_W1, L0_ffn_b1, L0_ffn_W2, L0_ffn_b2):
    import concourse.bacc as bacc
    from concourse.bass_utils import run_bass_kernel_spmd

    a = np.asarray
    heads = [a(w).reshape(NC, P, H, P).transpose(2, 1, 0, 3) for w in (L0_attn_Wq, L0_attn_Wk, L0_attn_Wv)]
    data = {
        "x": a(x).reshape(B * C, N), "ctx": a(ctx_2048), "ctx0T": a(ctx_2048)[:, 0:BANK, :].transpose(0, 2, 1), "conv_wT": a(L0_xattn_conv_w).T, "conv_b": a(L0_xattn_conv_b),
        "bn_gamma": a(L0_xattn_bn_gamma), "bn_beta": a(L0_xattn_bn_beta), "wqkv": np.stack(heads, axis=2),
        "wo": a(L0_attn_Wo),
        "lambdas": np.concatenate([a(L0_attn_lambda_q1), a(L0_attn_lambda_k1), a(L0_attn_lambda_q2), a(L0_attn_lambda_k2)]),
        "g": a(L0_attn_g), "w1t": a(L0_ffn_W1).T, "b1": a(L0_ffn_b1).reshape(HC, P).T, "w2t": a(L0_ffn_W2).T, "b2": a(L0_ffn_b2),
        "consts": constants(),
    }
    nc = bacc.Bacc("TRN2", target_bir_lowering=False, num_devices=1)
    arrays = {f"in_{n}": np.ascontiguousarray(data[n]) for n in _INS}
    aps = [nc.dram_tensor(f"in_{n}", arrays[f"in_{n}"].shape, mybir.dt.from_np(arrays[f"in_{n}"].dtype),
                          kind="ExternalInput").ap() for n in _INS]
    out = nc.dram_tensor("out", (B * C, N), F32, kind="ExternalOutput").ap()
    build(nc, *aps, out)
    r = run_bass_kernel_spmd(nc, [arrays], core_ids=[0])
    return r.results[0]["out"].reshape(B, C, N)
```
